# Optimizing a Trainium2 kernel written in Bass

```python
import numpy as np
import jax
import jax.numpy as jnp

def _softmax(x, axis=-1):
    return jax.nn.softmax(x, axis=axis)

def _gelu(x):
    return jax.nn.gelu(x, approximate=True)

def _silu(x):
    return jax.nn.silu(x)

def _sigmoid(x):
    return jax.nn.sigmoid(x)

def _layernorm(x, axis=-1, eps=1e-05):
    m = jnp.mean(x, axis=axis, keepdims=True)
    v = jnp.var(x, axis=axis, keepdims=True)
    return (x - m) / jnp.sqrt(v + eps)

def _scatter_add(tgt, idx, src, axis=0):
    return tgt.at[idx].add(src)

def _segment_sum(src, seg, n):
    return jax.ops.segment_sum(src, seg, n)
kernel_name = 'mk_gnn_resnorm_d1_gnn_r8_6d634c'

def setup_inputs(seed: int=0):
    np.random.seed(seed)
    _w = jnp.asarray

    def _rec_inputs():
        import jax
        import jax.numpy as jnp
        _gk = jax.random.key(seed)
        x = -0.000202 + 1 * jax.random.normal(jax.random.fold_in(_gk, 1), (12500, 64), jnp.float32)
        src = jax.random.randint(jax.random.fold_in(_gk, 2), (400000,), 0, 12500, jnp.int32)
        dst = jnp.minimum((12500 * jax.random.uniform(jax.random.fold_in(_gk, 3), (400000,)) ** 2.0).astype(jnp.int32), 99999)
        _o = jnp.argsort(dst, stable=True)
        src = src[_o]
        dst = dst[_o]
        edge_attr_64 = -8.47137e-05 + 0.99988 * jax.random.normal(jax.random.fold_in(_gk, 11), (400000, 64), jnp.float32)
        return (x, src, dst, edge_attr_64)
    x, src, dst, edge_attr_64 = _rec_inputs()

    def _L0_gnn_setup():
        import jax, jax.numpy as jnp
        import numpy as np
        D = 64
        N_ATOMS = 12500
        N_BONDS = 187500

        def _gated_mlp(x, W1, b1, W2, b2, G1, g1, G2, g2):
            h = jax.nn.silu(x @ W1 + b1)
            h = jax.nn.silu(h @ W2 + b2)
            g = jax.nn.silu(x @ G1 + g1)
            g = jax.nn.sigmoid(g @ G2 + g2)
            return h * g
        key = jax.random.key(seed)
        ks = jax.random.split(key, 8)
        s = 1.0 / np.sqrt(D)
        return {'atom_features': jax.random.normal(ks[0], (N_ATOMS, D), jnp.float32), 'bond_features': jax.random.normal(ks[1], (N_BONDS, D), jnp.float32), 'W1': jax.random.normal(ks[2], (D, D), jnp.float32) * s, 'b1': jnp.zeros((D,), jnp.float32), 'W2': jax.random.normal(ks[3], (D, D), jnp.float32) * s, 'b2': jnp.zeros((D,), jnp.float32), 'G1': jax.random.normal(ks[4], (D, D), jnp.float32) * s, 'g1': jnp.zeros((D,), jnp.float32), 'G2': jax.random.normal(ks[5], (D, D), jnp.float32) * s, 'g2': jnp.zeros((D,), jnp.float32), 'bond_atom_indices': jax.random.randint(ks[6], (N_BONDS, 2), 0, N_ATOMS, jnp.int32)}
    _L0_gnn_all = _L0_gnn_setup()
    _L0_gnn_in = {k: v for k, v in _L0_gnn_all.items() if k in ('W1', 'b1', 'W2', 'b2', 'G1', 'g1', 'G2', 'g2')}
    del _L0_gnn_all
    return {'x': x, 'src': src, 'dst': dst, 'edge_attr_64': edge_attr_64, 'L0_gnn_W1': _L0_gnn_in['W1'], 'L0_gnn_b1': _L0_gnn_in['b1'], 'L0_gnn_W2': _L0_gnn_in['W2'], 'L0_gnn_b2': _L0_gnn_in['b2'], 'L0_gnn_G1': _L0_gnn_in['G1'], 'L0_gnn_g1': _L0_gnn_in['g1'], 'L0_gnn_G2': _L0_gnn_in['G2'], 'L0_gnn_g2': _L0_gnn_in['g2']}

def reference(x, src, dst, edge_attr_64, L0_gnn_W1, L0_gnn_b1, L0_gnn_W2, L0_gnn_b2, L0_gnn_G1, L0_gnn_g1, L0_gnn_G2, L0_gnn_g2):
    import jax
    import jax.numpy as jnp

    def _L0_gnn_ref(atom_features, bond_features, W1, b1, W2, b2, G1, g1, G2, g2, bond_atom_indices):
        import jax, jax.numpy as jnp
        import numpy as np
        D = 64
        N_ATOMS = 12500
        N_BONDS = 187500

        def _gated_mlp(x, W1, b1, W2, b2, G1, g1, G2, g2):
            h = jax.nn.silu(x @ W1 + b1)
            h = jax.nn.silu(h @ W2 + b2)
            g = jax.nn.silu(x @ G1 + g1)
            g = jax.nn.sigmoid(g @ G2 + g2)
            return h * g
        messages = _gated_mlp(bond_features, W1, b1, W2, b2, G1, g1, G2, g2)
        recv = bond_atom_indices[:, 1]
        summed = jax.ops.segment_sum(messages, recv, num_segments=atom_features.shape[0])
        return atom_features + summed
    edge_index_t = jnp.stack([src, dst], axis=1)
    x = _layernorm(x + _L0_gnn_ref(x, edge_attr_64, L0_gnn_W1, L0_gnn_b1, L0_gnn_W2, L0_gnn_b2, L0_gnn_G1, L0_gnn_g1, L0_gnn_G2, L0_gnn_g2, edge_index_t), axis=-1)
    return x

_drawn_inputs = setup_inputs


def setup_inputs(seed=0):
    import zlib

    import numpy as np

    out = dict(_drawn_inputs(seed))
    spreads = {'L0_gnn_b1': (0.0, 0.1),
     'L0_gnn_b2': (0.0, 0.1),
     'L0_gnn_g1': (0.0, 0.327),
     'L0_gnn_g2': (0.0, 0.1)}
    factors = {}
    for name, (base, spread) in spreads.items():
        noise = np.random.default_rng([zlib.crc32(name.encode()), seed]).standard_normal(out[name].shape)
        drawn = base * np.exp(spread * noise) if base else spread * noise
        out[name] = jnp.asarray(drawn.astype(out[name].dtype))
    for name, factor in factors.items():
        out[name] = (out[name] * factor).astype(out[name].dtype)
    return out
```

```python
import numpy as np

import concourse.bass as bass
from concourse import mybir
from contextlib import ExitStack

P = 128
D = 64
NODES = 12500
EDGES = 400000
TILE = 128
TILES = 4
HALF = TILE * TILES
CHUNK = 2 * HALF
BODY = 4
CHUNKS = -(-EDGES // (CHUNK * BODY)) * BODY
HALVES = 2 * CHUNKS
HALF_ROWS = 112
HALF_COLS = HALVES // HALF_ROWS
WINDOW = 48
BLOCKS = -(-NODES // P)
NODES_PAD = BLOCKS * P
SUM_COLS = -(-NODES_PAD // WINDOW) * WINDOW
WINDOWS = SUM_COLS // WINDOW
LAST_BASE = SUM_COLS - WINDOW
FINAL = 7
FINALS = BLOCKS // FINAL
EPS = 1e-5
assert HALF_ROWS * HALF_COLS == HALVES and FINALS * FINAL == BLOCKS and CHUNKS % BODY == 0


def build(nc, x_nodes, x_edges, dst_halves, dst_tiles, w_first, w_second, b_first, b_second, out):
    fp32, bf16, i32 = mybir.dt.float32, mybir.dt.bfloat16, mybir.dt.int32
    ALU, ACT, AX = mybir.AluOpType, mybir.ActivationFunctionType, mybir.AxisListType

    with ExitStack() as ctx:
        def sb(name, shape, dt=fp32):
            return ctx.enter_context(nc.sbuf_tensor(name, shape, dt))

        def ps(name, shape):
            return ctx.enter_context(nc.psum_tensor(name, shape, fp32))

        def sem(name):
            return ctx.enter_context(nc.semaphore(name))

        w1g1 = sb("w1g1", [P, P])
        w2g2 = sb("w2g2", [P, D])
        b1g1 = sb("b1g1", [P, 1])
        bias_f = sb("bias_f", [P, 2, D])
        bias_rows = sb("bias_rows", [P, 2 * TILES, D])
        ones = sb("ones", [P, P])
        iota = sb("iota", [P, WINDOW])
        fold = sb("fold", [P, D])
        x_in = [sb(f"x_in{s}", [P, HALF]) for s in range(BODY)]
        hidden = [sb(f"hidden{s}", [P, 2, HALF]) for s in range(2)]
        silu = [sb(f"silu{s}", [P, 2 * TILES, D]) for s in range(2)]
        gate = [sb(f"gate{s}", [P, 2 * TILES, D]) for s in range(2)]
        msg = [sb(f"msg{s}", [P, 2 * TILES, D]) for s in range(2)]
        onehot = [sb(f"onehot{s}", [P, 2 * TILES, WINDOW]) for s in range(2)]
        dst_h = sb("dst_h", [HALF_ROWS, HALF_COLS, HALF], i32)
        least = sb("least", [HALF_ROWS, HALF_COLS])
        base_h = sb("base_h", [HALF_ROWS, HALF_COLS], i32)
        dst_t = sb("dst_t", [P, CHUNKS * 2, TILES], i32)
        base = sb("base", [P, HALVES], i32)
        rel = sb("rel", [P, CHUNKS * 2, TILES])
        sums = sb("sums", [P, SUM_COLS])
        x_n = sb("x_n", [P, BLOCKS, D])
        y = [sb(f"y{s}", [P, FINAL, D]) for s in range(2)]
        sq = [sb(f"sq{s}", [P, FINAL, D]) for s in range(2)]
        stat = sb("stat", [P, 4, BLOCKS])

        p_first = [ps(f"p_first{s}", [P, 2, HALF]) for s in range(2)]
        p_silu = ps("p_silu", [P, 2 * TILES, D])
        p_gate = ps("p_gate", [P, 2 * TILES, D])
        p_seg = [ps(f"p_seg{s}", [P, 512]) for s in range(2)]

        base_dram = nc.dram_tensor("base_scratch", (HALF_ROWS, HALF_COLS), i32, kind="Internal").ap()

        weights_in = sem("weights_in")
        x_loaded = [sem(f"x_loaded{s}") for s in range(BODY)]
        dst_h_in, dst_t_in = sem("dst_h_in"), sem("dst_t_in")
        base_out, base_in = sem("base_out"), sem("base_in")
        x_n_in = sem("x_n_in")
        consts = sem("consts")
        bias_ready = sem("bias_ready")
        least_step = sem("least_step")
        base_ready = sem("base_ready")
        rel_ready = sem("rel_ready")
        sums_zero = sem("sums_zero")
        first_done, hidden_ready = sem("first_done"), sem("hidden_ready")
        second_done = sem("second_done")
        silu_ready, gate_ready = sem("silu_ready"), sem("gate_ready")
        onehot_ready, msg_ready = sem("onehot_ready"), sem("msg_ready")
        seg_done, sums_added = sem("seg_done"), sem("sums_added")
        fold_done = sem("fold_done")
        y_ready, mean_ready, centred = sem("y_ready"), sem("mean_ready"), sem("centred")
        squared, var_ready, std_ready = sem("squared"), sem("var_ready"), sem("std_ready")
        var_ready_step = sem("var_sum_ready")
        rstd_ready, normed = sem("rstd_ready"), sem("normed")
        stored = sem("stored")

        block = ctx.enter_context(nc.Block())

        @block.sync
        def _(sp):
            sp.dma_start(x_in[0][:, :], x_edges[:, 0, :]).then_inc(x_loaded[0], 16)
            for c in range(1, BODY):
                sp.dma_start(x_in[c][:, :], x_edges[:, c, :]).then_inc(x_loaded[c], 16)
            with sp.Fori(1, CHUNKS // BODY) as j:
                for s in range(BODY):
                    sp.wait_ge(first_done, j * BODY + (s + 1 - BODY))
                    sp.dma_start(x_in[s][:, :], x_edges[:, bass.ds(j * BODY + s, 1), :].rearrange("p a n -> p (a n)"))\
                      .then_inc(x_loaded[s], 16)
            sp.dma_start(x_n[:, :, :], x_nodes).then_inc(x_n_in, 16)
            for f in range(FINALS):
                sp.wait_ge(normed, f + 1)
                sp.dma_start(out[:, f * FINAL:(f + 1) * FINAL, :], x_n[:, f * FINAL:(f + 1) * FINAL, :])\
                  .then_inc(stored, 16)
            sp.wait_ge(stored, 16 * FINALS)

        @block.gpsimd
        def _(pool):
            pool.memset(ones[:, :], 1.0).then_inc(consts, 1)
            pool.iota(iota[:, :], [[1, WINDOW]], base=0, channel_multiplier=0,
                      allow_small_or_imprecise_dtypes=True).then_inc(consts, 1)
            pool.memset(fold[:, :], 0.0).then_inc(consts, 1)
            pool.wait_ge(consts, 3)
            for h in range(2):
                pool.affine_select(out=fold[:, :], in_=fold[:, :], compare_op=ALU.not_equal, fill=0.5,
                                   base=-D * h, pattern=[[-1, D]], channel_multiplier=1).then_inc(consts, 1)
                pool.wait_ge(consts, 4 + h)
            pool.memset(sums[:, :], 0.0).then_inc(sums_zero, 1)
            for f in range(FINALS):
                pool.wait_ge(centred, f + 1)
                if f >= 2:
                    pool.wait_ge(var_ready, f - 1)
                pool.tensor_tensor(sq[f % 2][:, :, :], y[f % 2][:, :, :], y[f % 2][:, :, :], ALU.mult)\
                    .then_inc(squared, 1)

        @block.scalar
        def _(act):
            act.dma_start(w1g1[:, :], w_first).then_inc(weights_in, 16)
            act.dma_start(b1g1[:, :], b_first).then_inc(weights_in, 16)
            act.dma_start(w2g2[:, :], w_second).then_inc(weights_in, 16)
            act.dma_start(bias_rows[:, :, :], b_second).then_inc(weights_in, 16)
            act.dma_start(dst_h[:, :, :], dst_halves).then_inc(dst_h_in, 16)
            act.dma_start(dst_t[:, :, :], dst_tiles).then_inc(dst_t_in, 16)
            act.wait_ge(base_ready, 1)
            act.dma_start(base_dram, base_h[:, :]).then_inc(base_out, 16)
            act.wait_ge(base_out, 16)
            act.dma_start(base[:, :], base_dram.rearrange("a b -> (a b)").partition_broadcast(P))\
               .then_inc(base_in, 16)
            act.wait_ge(weights_in, 64)

            def first(c, s, wait_free=True):
                act.wait_ge(first_done, c + 1)
                if wait_free:
                    act.wait_ge(second_done, c - 1)
                act.activation(hidden[s % 2][:, :, :], p_first[s % 2][:, :, :], ACT.Silu, bias=b1g1[:, 0:1])\
                   .then_inc(hidden_ready, 1)

            def second(c, s, wait_free=True):
                act.wait_ge(second_done, c + 1)
                if wait_free:
                    act.wait_ge(msg_ready, c - 1)
                act.activation(silu[s % 2][:, :, :], p_silu[:, :, :], ACT.Silu).then_inc(silu_ready, 1)
                act.activation(gate[s % 2][:, :, :], p_gate[:, :, :], ACT.Tanh, scale=0.5).then_inc(gate_ready, 1)

            first(0, 0, False)
            for c in range(BODY):
                first(c + 1, c + 1, c >= 1)
                second(c, c, c >= 2)
            with act.Fori(1, CHUNKS // BODY - 1) as j:
                for s in range(BODY):
                    first(j * BODY + (s + 1), s + 1)
                    second(j * BODY + s, s)
            for c in range(CHUNKS - BODY, CHUNKS):
                if c + 1 < CHUNKS:
                    first(c + 1, c + 1)
                second(c, c)
            for f in range(FINALS):
                act.wait_ge(var_ready, f + 1)
                act.activation(stat[:, 2, f * FINAL:(f + 1) * FINAL], stat[:, 1, f * FINAL:(f + 1) * FINAL], ACT.Sqrt)\
                   .then_inc(std_ready, 1)

        @block.vector
        def _(dve):
            dve.wait_ge(dst_h_in, 16)
            dve.tensor_reduce(least[:, :], dst_h[:, :, :], AX.X, ALU.min).then_inc(least_step, 1)
            dve.wait_ge(least_step, 1)
            dve.tensor_scalar(base_h[:, :], least[:, :], 0.0, float(LAST_BASE), ALU.max, ALU.min)\
               .then_inc(base_ready, 1)
            dve.wait_ge(dst_t_in, 16)
            dve.wait_ge(base_in, 16)
            dve.tensor_tensor(rel[:, :, :], dst_t[:, :, :],
                              base[:, :].rearrange("p (h o) -> p h o", o=1).broadcast_to([P, HALVES, TILES]),
                              ALU.subtract).then_inc(rel_ready, 1)
            dve.wait_ge(rel_ready, 1)
            dve.wait_ge(consts, 5)
            dve.wait_ge(sums_zero, 1)

            def message(c, s, wait_free=True):
                if wait_free:
                    dve.wait_ge(seg_done, c - 1)
                dve.tensor_tensor(onehot[s % 2][:, :, :],
                                  iota[:, :].rearrange("p (o w) -> p o w", o=1).broadcast_to([P, 2 * TILES, WINDOW]),
                                  rel[:, bass.ds(c * 2, 2), :].rearrange("p h (i o) -> p (h i) o", o=1)
                                  .broadcast_to([P, 2 * TILES, WINDOW]),
                                  ALU.is_equal).then_inc(onehot_ready, 1)
                dve.wait_ge(silu_ready, c + 1)
                dve.wait_ge(gate_ready, c + 1)
                dve.scalar_tensor_tensor(msg[s % 2][:, :, :], gate[s % 2][:, :, :], 1.0, silu[s % 2][:, :, :],
                                         ALU.add, ALU.mult).then_inc(msg_ready, 1)

            def add(c, s, wait_last=True):
                starts = [dve.value_load(base[0:1, bass.ds(c * 2 + h, 1)], min_val=0, max_val=LAST_BASE)
                          for h in range(2)]
                dve.wait_ge(seg_done, c + 1)
                if wait_last:
                    dve.wait_ge(sums_added, 2 * c)
                for h in range(2):
                    rows = slice(D * h, D * h + D)
                    dve.tensor_tensor(sums[rows, bass.ds(starts[h], WINDOW)], sums[rows, bass.ds(starts[h], WINDOW)],
                                      p_seg[s % 2][rows, 0:WINDOW], ALU.add).then_inc(sums_added, 1)

            message(0, 0, False)
            for c in range(1, BODY):
                message(c, c, c >= 2)
                add(c - 1, c - 1, c >= 2)
            with dve.Fori(1, CHUNKS // BODY) as j:
                for s in range(BODY):
                    message(j * BODY + s, s)
                    add(j * BODY + (s - 1), s - 1)
            add(CHUNKS - 1, CHUNKS - 1)

            dve.wait_ge(x_n_in, 16)
            def spread(row, f):
                return stat[:, row, f * FINAL:(f + 1) * FINAL].rearrange("p (b o) -> p b o", o=1)\
                    .broadcast_to([P, FINAL, D])

            def centre(f):
                cols = slice(f * FINAL, (f + 1) * FINAL)
                yf = y[f % 2]
                dve.wait_ge(fold_done, f + 1)
                if f >= 2:
                    dve.wait_ge(squared, f - 1)
                    dve.wait_ge(normed, f - 1)
                dve.scalar_tensor_tensor(yf[:, :, :], x_n[:, cols, :], 2.0,
                                         p_seg[f % 2][:, 0:FINAL * D].rearrange("p (b d) -> p b d", d=D),
                                         ALU.mult, ALU.add).then_inc(y_ready, 1)
                dve.wait_ge(y_ready, f + 1)
                dve.tensor_reduce(stat[:, 0, cols], yf[:, :, :], AX.X, ALU.add).then_inc(mean_ready, 1)
                dve.wait_ge(mean_ready, 2 * f + 1)
                dve.tensor_scalar(stat[:, 3, cols], stat[:, 0, cols], 1.0 / D, None, ALU.mult).then_inc(mean_ready, 1)
                dve.wait_ge(mean_ready, 2 * f + 2)
                dve.tensor_tensor(yf[:, :, :], yf[:, :, :], spread(3, f), ALU.subtract).then_inc(centred, 1)

            def norm(f):
                cols = slice(f * FINAL, (f + 1) * FINAL)
                yf = y[f % 2]
                dve.wait_ge(squared, f + 1)
                dve.tensor_reduce(stat[:, 0, cols], sq[f % 2][:, :, :], AX.X, ALU.add).then_inc(var_ready_step, 1)
                dve.wait_ge(var_ready_step, f + 1)
                dve.tensor_scalar(stat[:, 1, cols], stat[:, 0, cols], 1.0 / D, EPS, ALU.mult, ALU.add)\
                   .then_inc(var_ready, 1)
                dve.wait_ge(std_ready, f + 1)
                dve.reciprocal(stat[:, 3, cols], stat[:, 2, cols]).then_inc(rstd_ready, 1)
                dve.wait_ge(rstd_ready, f + 1)
                dve.tensor_tensor(x_n[:, cols, :], yf[:, :, :], spread(3, f), ALU.mult).then_inc(normed, 1)

            for f in range(FINALS):
                centre(f)
                norm(f)

        @block.tensor
        def _(pe):
            pe.wait_ge(weights_in, 64)
            pe.wait_ge(consts, 5)

            def first(c, s, loads, wait_free=True):
                pe.wait_ge(x_loaded[s % BODY], loads)
                if wait_free:
                    pe.wait_ge(hidden_ready, c - 1)
                for h in range(2):
                    rows = slice(D * h, D * h + D)
                    last = pe.matmul(p_first[s % 2][:, h, :], w1g1[rows, :], x_in[s % BODY][rows, :],
                                     start=True, stop=True)
                last.then_inc(first_done, 1)

            def second(c, s, wait_free=True):
                pe.wait_ge(hidden_ready, c + 1)
                if wait_free:
                    pe.wait_ge(silu_ready, c)
                    pe.wait_ge(gate_ready, c)
                for k, bank in enumerate((p_silu, p_gate)):
                    row = slice(D * k, D * k + D)
                    pe.matmul(bank[:, :, :], ones[D * k:D * k + 1, :], bias_rows[D * k:D * k + 1, :, :],
                              start=True, stop=False, skip_group_check=True)
                for t in range(2 * TILES):
                    h, i = divmod(t, TILES)
                    for k, bank in enumerate((p_silu, p_gate)):
                        rows = slice(D * k, D * k + D)
                        last = pe.matmul(bank[:, t, :], hidden[s % 2][rows, h, i * TILE:(i + 1) * TILE],
                                         w2g2[rows, :], start=False, stop=True, skip_group_check=True)
                last.then_inc(second_done, 1)

            def segment(c, s, wait_free=True):
                pe.wait_ge(onehot_ready, c + 1)
                pe.wait_ge(msg_ready, c + 1)
                if wait_free:
                    pe.wait_ge(sums_added, 2 * c - 2)
                for i in range(TILES):
                    for h in range(2):
                        t = h * TILES + i
                        last = pe.matmul(p_seg[s % 2][D * h:D * h + D, 0:WINDOW], msg[s % 2][:, t, :],
                                         onehot[s % 2][:, t, :], start=(i == 0), stop=(i == TILES - 1),
                                         skip_group_check=True)
                last.then_inc(seg_done, 1)

            first(0, 0, 16, False)
            first(1, 1, 16, False)
            second(0, 0, False)
            for c in range(BODY):
                first(c + 2, c + 2, 16 * ((c + 2) // BODY + 1))
                second(c + 1, c + 1)
                segment(c, c, c >= 2)
            with pe.Fori(1, CHUNKS // BODY - 1) as j:
                for s in range(BODY):
                    first(j * BODY + (s + 2), s + 2, j * 16 + 16 * ((s + 2) // BODY + 1))
                    second(j * BODY + (s + 1), s + 1)
                    segment(j * BODY + s, s)
            for c in range(CHUNKS - BODY, CHUNKS):
                if c + 2 < CHUNKS:
                    first(c + 2, c + 2, 16 * ((c + 2) // BODY + 1))
                if c + 1 < CHUNKS:
                    second(c + 1, c + 1)
                segment(c, c)
            pe.wait_ge(sums_added, 2 * CHUNKS)
            for f in range(FINALS):
                if f >= 2:
                    pe.wait_ge(y_ready, f - 1)
                for b in range(FINAL):
                    n = f * FINAL + b
                    last = pe.matmul(p_seg[f % 2][:, b * D:(b + 1) * D], sums[:, n * P:(n + 1) * P], fold[:, :],
                                     start=True, stop=True, skip_group_check=True)
                last.then_inc(fold_done, 1)


def kernel(x, src, dst, edge_attr_64, L0_gnn_W1, L0_gnn_b1, L0_gnn_W2, L0_gnn_b2,
           L0_gnn_G1, L0_gnn_g1, L0_gnn_G2, L0_gnn_g2):
    import concourse.bacc as bacc
    from concourse.bass_utils import run_bass_kernel_spmd

    f32 = np.float32
    e = np.zeros((CHUNKS * CHUNK, D), f32)
    e[:EDGES] = np.asarray(edge_attr_64)
    d = np.full((CHUNKS * CHUNK,), NODES, np.int32)
    d[:EDGES] = np.asarray(dst)
    n = np.zeros((NODES_PAD, D), f32)
    n[:NODES] = np.asarray(x)
    w1g1 = np.concatenate([np.asarray(L0_gnn_W1), np.asarray(L0_gnn_G1)], 1)
    bias2 = np.zeros((P, 2 * TILES, D), f32)
    bias2[0], bias2[D] = np.asarray(L0_gnn_b2), np.asarray(L0_gnn_g2)
    arrays = {
        "x_nodes": n.reshape(BLOCKS, P, D).transpose(1, 0, 2),
        "x_edges": e.reshape(CHUNKS, 2, HALF, D).transpose(1, 3, 0, 2).reshape(P, CHUNKS, HALF),
        "dst_halves": d.reshape(HALF_ROWS, HALF_COLS, HALF),
        "dst_tiles": d.reshape(HALVES, TILES, TILE).transpose(2, 0, 1),
        "w_first": np.concatenate([w1g1, w1g1], 0),
        "w_second": np.concatenate([np.asarray(L0_gnn_W2), np.asarray(L0_gnn_G2)], 0),
        "b_first": np.concatenate([np.asarray(L0_gnn_b1), np.asarray(L0_gnn_g1)]).reshape(P, 1),
        "b_second": bias2,
    }
    arrays = {k: np.ascontiguousarray(v) for k, v in arrays.items()}
    nc = bacc.Bacc("TRN2", target_bir_lowering=False, num_devices=1)
    args = [nc.dram_tensor(k, v.shape, mybir.dt.from_np(v.dtype), kind="ExternalInput").ap()
            for k, v in arrays.items()]
    out = nc.dram_tensor("out", (P, BLOCKS, D), mybir.dt.float32, kind="ExternalOutput").ap()
    build(nc, *args, out)
    r = run_bass_kernel_spmd(nc, [arrays], core_ids=[0])
    return np.ascontiguousarray(r.results[0]["out"].transpose(1, 0, 2).reshape(NODES_PAD, D)[:NODES])
```

```python
import numpy as np

import concourse.bass as bass
from concourse import mybir
from contextlib import ExitStack

P = 128
D = 64
NODES = 12500
EDGES = 400000
TILE = 128
TILES = 4
HALF = TILE * TILES
CHUNK = 2 * HALF
BODY = 4
CHUNKS = -(-EDGES // (CHUNK * BODY)) * BODY
HALVES = 2 * CHUNKS
HALF_ROWS = 112
HALF_COLS = HALVES // HALF_ROWS
WINDOW = 48
BLOCKS = -(-NODES // P)
NODES_PAD = BLOCKS * P
SUM_COLS = -(-NODES_PAD // WINDOW) * WINDOW
WINDOWS = SUM_COLS // WINDOW
LAST_BASE = SUM_COLS - WINDOW
FINAL = 7
FINALS = BLOCKS // FINAL
EPS = 1e-5
assert HALF_ROWS * HALF_COLS == HALVES and FINALS * FINAL == BLOCKS and CHUNKS % BODY == 0


def build(nc, x_nodes, x_edges, dst_halves, dst_tiles, w_first, w_second, b_first, b_second, out):
    fp32, bf16, i32 = mybir.dt.float32, mybir.dt.bfloat16, mybir.dt.int32
    ALU, ACT, AX = mybir.AluOpType, mybir.ActivationFunctionType, mybir.AxisListType

    with ExitStack() as ctx:
        def sb(name, shape, dt=fp32):
            return ctx.enter_context(nc.sbuf_tensor(name, shape, dt))

        def ps(name, shape):
            return ctx.enter_context(nc.psum_tensor(name, shape, fp32))

        def sem(name):
            return ctx.enter_context(nc.semaphore(name))

        w1g1 = sb("w1g1", [P, 2, P])
        w2g2 = sb("w2g2", [P, P])
        b1g1 = sb("b1g1", [P, 1])
        bias_in = sb("bias_in", [1, P])
        bias_rest = sb("bias_rest", [1, 2, P])
        bias_part = sb("bias_part", [1, 3, P], bf16)
        bias_rows = sb("bias_rows", [P, TILES, P], bf16)
        ones = sb("ones", [P, P], bf16)
        iota = sb("iota", [P, WINDOW])
        fold = sb("fold", [P, D])
        x_in = [sb(f"x_in{s}", [P, HALF]) for s in range(BODY)]
        hidden = [sb(f"hidden{s}", [P, 2, HALF]) for s in range(2)]
        silu = [sb(f"silu{s}", [P, 2 * TILES, D]) for s in range(2)]
        gate = [sb(f"gate{s}", [P, 2 * TILES, D]) for s in range(2)]
        msg = [sb(f"msg{s}", [P, 2 * TILES, 2, D]) for s in range(2)]
        msg_low = [sb(f"msg_low{s}", [P, 2 * TILES, 2, D], bf16) for s in range(2)]
        onehot = [sb(f"onehot{s}", [P, 2 * TILES, WINDOW], bf16) for s in range(2)]
        dst_h = sb("dst_h", [HALF_ROWS, HALF_COLS, HALF], i32)
        least = sb("least", [HALF_ROWS, HALF_COLS])
        base_h = sb("base_h", [HALF_ROWS, HALF_COLS], i32)
        dst_t = sb("dst_t", [P, CHUNKS * 2, TILES], i32)
        base = sb("base", [P, HALVES], i32)
        rel = sb("rel", [P, CHUNKS * 2, TILES])
        sums = sb("sums", [P, SUM_COLS])
        x_n = sb("x_n", [P, BLOCKS, D])
        y = [sb(f"y{s}", [P, FINAL, D]) for s in range(2)]
        sq = [sb(f"sq{s}", [P, FINAL, D]) for s in range(2)]
        stat = sb("stat", [P, 4, BLOCKS])

        p_first = [ps(f"p_first{s}", [P, 2, HALF]) for s in range(2)]
        p_second = ps("p_second", [P, 2 * TILES, 2, D])
        p_seg = [ps(f"p_seg{s}", [P, 512]) for s in range(2)]

        base_dram = nc.dram_tensor("base_scratch", (HALF_ROWS, HALF_COLS), i32, kind="Internal").ap()

        weights_in = sem("weights_in")
        x_loaded = [sem(f"x_loaded{s}") for s in range(BODY)]
        bias_in_sem = sem("bias_loaded")
        dst_h_in, dst_t_in = sem("dst_h_in"), sem("dst_t_in")
        base_out, base_in = sem("base_out"), sem("base_in")
        x_n_in = sem("x_n_in")
        consts = sem("consts")
        bias_step, bias_moved, bias_ready = sem("bias_step"), sem("bias_moved"), sem("bias_ready")
        weights_zero = sem("weights_zero")
        msg_low_zero = sem("msg_low_zero")
        rest_ready, low_ready = sem("rest_ready"), sem("low_ready")
        least_step = sem("least_step")
        base_ready = sem("base_ready")
        rel_ready = sem("rel_ready")
        sums_zero = sem("sums_zero")
        first_done, hidden_ready = sem("first_done"), sem("hidden_ready")
        second_done = sem("second_done")
        silu_ready, gate_ready = sem("silu_ready"), sem("gate_ready")
        onehot_ready, msg_ready = sem("onehot_ready"), sem("msg_ready")
        seg_done, sums_added = sem("seg_done"), sem("sums_added")
        fold_done = sem("fold_done")
        y_ready, mean_ready, centred = sem("y_ready"), sem("mean_ready"), sem("centred")
        squared, var_ready, std_ready = sem("squared"), sem("var_ready"), sem("std_ready")
        var_ready_step = sem("var_sum_ready")
        rstd_ready, normed = sem("rstd_ready"), sem("normed")
        stored = sem("stored")

        block = ctx.enter_context(nc.Block())

        @block.sync
        def _(sp):
            sp.dma_start(x_in[0][:, :], x_edges[:, 0, :]).then_inc(x_loaded[0], 16)
            for c in range(1, BODY):
                sp.dma_start(x_in[c][:, :], x_edges[:, c, :]).then_inc(x_loaded[c], 16)
            sp.wait_ge(bias_step, 6)
            for k in range(3):
                for i in range(TILES):
                    sp.dma_start(bias_rows[k:k + 1, i, :], bias_part[0:1, k, :]).then_inc(bias_moved, 16)
            with sp.Fori(1, CHUNKS // BODY) as j:
                for s in range(BODY):
                    sp.wait_ge(first_done, j * BODY + (s + 1 - BODY))
                    sp.dma_start(x_in[s][:, :], x_edges[:, bass.ds(j * BODY + s, 1), :].rearrange("p a n -> p (a n)"))\
                      .then_inc(x_loaded[s], 16)
            sp.dma_start(x_n[:, :, :], x_nodes).then_inc(x_n_in, 16)
            for f in range(FINALS):
                sp.wait_ge(normed, f + 1)
                sp.dma_start(out[:, f * FINAL:(f + 1) * FINAL, :], x_n[:, f * FINAL:(f + 1) * FINAL, :])\
                  .then_inc(stored, 16)
            sp.wait_ge(stored, 16 * FINALS)

        @block.gpsimd
        def _(pool):
            pool.memset(ones[:, :], 1.0).then_inc(consts, 1)
            pool.iota(iota[:, :], [[1, WINDOW]], base=0, channel_multiplier=0,
                      allow_small_or_imprecise_dtypes=True).then_inc(consts, 1)
            pool.memset(fold[:, :], 0.0).then_inc(consts, 1)
            pool.wait_ge(consts, 3)
            for h in range(2):
                pool.affine_select(out=fold[:, :], in_=fold[:, :], compare_op=ALU.not_equal, fill=0.5,
                                   base=-D * h, pattern=[[-1, D]], channel_multiplier=1).then_inc(consts, 1)
                pool.wait_ge(consts, 4 + h)
            pool.memset(sums[:, :], 0.0).then_inc(sums_zero, 1)
            for s in range(2):
                pool.memset(msg_low[s][:, :, :, :], 0.0).then_inc(msg_low_zero, 1)
            pool.wait_ge(msg_low_zero, 2)

            def upper(ap):
                return ap.bitcast(bf16).rearrange("p t (d two) -> p t d two", two=2)[:, :, :, 1]

            def split(c, s):
                pool.wait_ge(msg_ready, c + 1)
                whole, rest = msg[s % 2][:, :, 0, :], msg[s % 2][:, :, 1, :]
                pool.tensor_tensor(rest, whole, upper(whole), ALU.subtract).then_inc(rest_ready, 1)
                pool.wait_ge(rest_ready, c + 1)
                pool.tensor_tensor(msg_low[s % 2][:, :, 0, :], rest, upper(rest), ALU.subtract)\
                    .then_inc(low_ready, 1)

            with pool.Fori(0, CHUNKS // BODY) as j:
                for s in range(BODY):
                    split(j * BODY + s, s)
            for f in range(FINALS):
                pool.wait_ge(centred, f + 1)
                if f >= 2:
                    pool.wait_ge(var_ready, f - 1)
                pool.tensor_tensor(sq[f % 2][:, :, :], y[f % 2][:, :, :], y[f % 2][:, :, :], ALU.mult)\
                    .then_inc(squared, 1)

        @block.scalar
        def _(act):
            act.dma_start(b1g1[:, :], b_first).then_inc(weights_in, 16)
            act.dma_start(bias_in[:, :], b_second).then_inc(bias_in_sem, 16)
            act.wait_ge(weights_zero, 2)
            for h in range(2):
                rows = slice(D * h, D * h + D)
                act.dma_start(w1g1[rows, h, :], w_first).then_inc(weights_in, 16)
                act.dma_start(w2g2[rows, rows], w_second[rows, :]).then_inc(weights_in, 16)
            act.dma_start(dst_h[:, :, :], dst_halves).then_inc(dst_h_in, 16)
            act.dma_start(dst_t[:, :, :], dst_tiles).then_inc(dst_t_in, 16)
            act.wait_ge(base_ready, 1)
            act.dma_start(base_dram, base_h[:, :]).then_inc(base_out, 16)
            act.wait_ge(base_out, 16)
            act.dma_start(base[:, :], base_dram.rearrange("a b -> (a b)").partition_broadcast(P))\
               .then_inc(base_in, 16)
            act.wait_ge(weights_in, 80)

            def first(c, s, wait_free=True):
                act.wait_ge(first_done, c + 1)
                if wait_free:
                    act.wait_ge(second_done, c - 1)
                act.activation(hidden[s % 2][:, :, :], p_first[s % 2][:, :, :], ACT.Silu, bias=b1g1[:, 0:1])\
                   .then_inc(hidden_ready, 1)

            def second(c, s, wait_free=True):
                act.wait_ge(second_done, c + 1)
                if wait_free:
                    act.wait_ge(msg_ready, c - 1)
                act.activation(silu[s % 2][:, :, :], p_second[:, :, 0, :], ACT.Silu).then_inc(silu_ready, 1)
                act.activation(gate[s % 2][:, :, :], p_second[:, :, 1, :], ACT.Tanh, scale=0.5).then_inc(gate_ready, 1)

            first(0, 0, False)
            for c in range(BODY):
                first(c + 1, c + 1, c >= 1)
                second(c, c, c >= 2)
            with act.Fori(1, CHUNKS // BODY - 1) as j:
                for s in range(BODY):
                    first(j * BODY + (s + 1), s + 1)
                    second(j * BODY + s, s)
            for c in range(CHUNKS - BODY, CHUNKS):
                if c + 1 < CHUNKS:
                    first(c + 1, c + 1)
                second(c, c)
            for f in range(FINALS):
                act.wait_ge(var_ready, f + 1)
                act.activation(stat[:, 2, f * FINAL:(f + 1) * FINAL], stat[:, 1, f * FINAL:(f + 1) * FINAL], ACT.Sqrt)\
                   .then_inc(std_ready, 1)

        @block.vector
        def _(dve):
            dve.memset(w1g1[:, :, :], 0.0).then_inc(weights_zero, 1)
            dve.memset(w2g2[:, :], 0.0).then_inc(weights_zero, 1)
            dve.memset(bias_rows[:, :, :], 0.0).then_inc(bias_step, 1)
            dve.wait_ge(bias_in_sem, 16)
            whole = bias_in[:, :]
            for k in range(3):
                dve.tensor_copy(bias_part[:, k, :], whole).then_inc(bias_step, 1)
                dve.wait_ge(bias_step, 2 * k + 2)
                if k < 2:
                    dve.tensor_tensor(bias_rest[:, k, :], whole, bias_part[:, k, :], ALU.subtract)\
                       .then_inc(bias_step, 1)
                    dve.wait_ge(bias_step, 2 * k + 3)
                    whole = bias_rest[:, k, :]
            dve.wait_ge(dst_h_in, 16)
            dve.tensor_reduce(least[:, :], dst_h[:, :, :], AX.X, ALU.min).then_inc(least_step, 1)
            dve.wait_ge(least_step, 1)
            dve.tensor_scalar(base_h[:, :], least[:, :], 0.0, float(LAST_BASE), ALU.max, ALU.min)\
               .then_inc(base_ready, 1)
            dve.wait_ge(dst_t_in, 16)
            dve.wait_ge(base_in, 16)
            dve.tensor_tensor(rel[:, :, :], dst_t[:, :, :],
                              base[:, :].rearrange("p (h o) -> p h o", o=1).broadcast_to([P, HALVES, TILES]),
                              ALU.subtract).then_inc(rel_ready, 1)
            dve.wait_ge(rel_ready, 1)
            dve.wait_ge(consts, 5)
            dve.wait_ge(sums_zero, 1)

            def message(c, s, wait_free=True):
                if wait_free:
                    dve.wait_ge(seg_done, c - 1)
                dve.tensor_tensor(onehot[s % 2][:, :, :],
                                  iota[:, :].rearrange("p (o w) -> p o w", o=1).broadcast_to([P, 2 * TILES, WINDOW]),
                                  rel[:, bass.ds(c * 2, 2), :].rearrange("p h (i o) -> p (h i) o", o=1)
                                  .broadcast_to([P, 2 * TILES, WINDOW]),
                                  ALU.is_equal).then_inc(onehot_ready, 1)
                dve.wait_ge(silu_ready, c + 1)
                dve.wait_ge(gate_ready, c + 1)
                dve.scalar_tensor_tensor(msg[s % 2][:, :, 0, :], gate[s % 2][:, :, :], 1.0, silu[s % 2][:, :, :],
                                         ALU.add, ALU.mult).then_inc(msg_ready, 1)

            def add(c, s, wait_last=True):
                starts = [dve.value_load(base[0:1, bass.ds(c * 2 + h, 1)], min_val=0, max_val=LAST_BASE)
                          for h in range(2)]
                dve.wait_ge(seg_done, c + 1)
                for h in range(2):
                    if h or wait_last:
                        dve.wait_ge(sums_added, c * 2 + h)
                    dve.tensor_tensor(sums[:, bass.ds(starts[h], WINDOW)], sums[:, bass.ds(starts[h], WINDOW)],
                                      p_seg[s % 2][:, h * WINDOW:(h + 1) * WINDOW], ALU.add)\
                       .then_inc(sums_added, 1)

            message(0, 0, False)
            for c in range(1, BODY):
                message(c, c, c >= 2)
                add(c - 1, c - 1, c >= 2)
            with dve.Fori(1, CHUNKS // BODY) as j:
                for s in range(BODY):
                    message(j * BODY + s, s)
                    add(j * BODY + (s - 1), s - 1)
            add(CHUNKS - 1, CHUNKS - 1)

            dve.wait_ge(x_n_in, 16)
            def spread(row, f):
                return stat[:, row, f * FINAL:(f + 1) * FINAL].rearrange("p (b o) -> p b o", o=1)\
                    .broadcast_to([P, FINAL, D])

            def centre(f):
                cols = slice(f * FINAL, (f + 1) * FINAL)
                yf = y[f % 2]
                dve.wait_ge(fold_done, f + 1)
                if f >= 2:
                    dve.wait_ge(squared, f - 1)
                    dve.wait_ge(normed, f - 1)
                dve.scalar_tensor_tensor(yf[:, :, :], x_n[:, cols, :], 2.0,
                                         p_seg[f % 2][:, 0:FINAL * D].rearrange("p (b d) -> p b d", d=D),
                                         ALU.mult, ALU.add).then_inc(y_ready, 1)
                dve.wait_ge(y_ready, f + 1)
                dve.tensor_reduce(stat[:, 0, cols], yf[:, :, :], AX.X, ALU.add).then_inc(mean_ready, 1)
                dve.wait_ge(mean_ready, 2 * f + 1)
                dve.tensor_scalar(stat[:, 3, cols], stat[:, 0, cols], 1.0 / D, None, ALU.mult).then_inc(mean_ready, 1)
                dve.wait_ge(mean_ready, 2 * f + 2)
                dve.tensor_tensor(yf[:, :, :], yf[:, :, :], spread(3, f), ALU.subtract).then_inc(centred, 1)

            def norm(f):
                cols = slice(f * FINAL, (f + 1) * FINAL)
                yf = y[f % 2]
                dve.wait_ge(squared, f + 1)
                dve.tensor_reduce(stat[:, 0, cols], sq[f % 2][:, :, :], AX.X, ALU.add).then_inc(var_ready_step, 1)
                dve.wait_ge(var_ready_step, f + 1)
                dve.tensor_scalar(stat[:, 1, cols], stat[:, 0, cols], 1.0 / D, EPS, ALU.mult, ALU.add)\
                   .then_inc(var_ready, 1)
                dve.wait_ge(std_ready, f + 1)
                dve.reciprocal(stat[:, 3, cols], stat[:, 2, cols]).then_inc(rstd_ready, 1)
                dve.wait_ge(rstd_ready, f + 1)
                dve.tensor_tensor(x_n[:, cols, :], yf[:, :, :], spread(3, f), ALU.mult).then_inc(normed, 1)

            for f in range(FINALS):
                centre(f)
                norm(f)

        @block.tensor
        def _(pe):
            pe.wait_ge(weights_in, 80)
            pe.wait_ge(consts, 5)
            pe.wait_ge(bias_moved, 48 * TILES)

            def first(c, s, loads, wait_free=True):
                pe.wait_ge(x_loaded[s % BODY], loads)
                if wait_free:
                    pe.wait_ge(hidden_ready, c - 1)
                for h in range(2):
                    last = pe.matmul(p_first[s % 2][:, h, :], w1g1[:, h, :], x_in[s % BODY][:, :],
                                     start=True, stop=True)
                last.then_inc(first_done, 1)

            def second(c, s, wait_free=True):
                pe.wait_ge(hidden_ready, c + 1)
                if wait_free:
                    pe.wait_ge(silu_ready, c)
                    pe.wait_ge(gate_ready, c)
                for h in range(2):
                    pe.matmul(p_second[:, h * TILES:(h + 1) * TILES, :, :], ones[:, :], bias_rows[:, :, :],
                              start=True, stop=False, skip_group_check=True)
                for t in range(2 * TILES):
                    h, i = divmod(t, TILES)
                    last = pe.matmul(p_second[:, t, :, :], hidden[s % 2][:, h, i * TILE:(i + 1) * TILE],
                                     w2g2[:, :], start=False, stop=True, skip_group_check=True)
                last.then_inc(second_done, 1)

            def segment(c, s, wait_free=True):
                pe.wait_ge(onehot_ready, c + 1)
                pe.wait_ge(low_ready, c + 1)
                if wait_free:
                    pe.wait_ge(sums_added, 2 * c - 2)
                for h in range(2):
                    window = p_seg[s % 2][:, h * WINDOW:(h + 1) * WINDOW]
                    for i in range(TILES):
                        t = h * TILES + i
                        parts = msg[s % 2][:, t, :, :].rearrange("p k d -> p (k d)").bitcast(bf16)\
                            .rearrange("p (d two) -> p d two", two=2)[:, :, 1]
                        pe.matmul(window, parts, onehot[s % 2][:, t, :], start=(i == 0), stop=False,
                                  skip_group_check=True)
                        last = pe.matmul(window, msg_low[s % 2][:, t, :, :], onehot[s % 2][:, t, :],
                                         start=False, stop=(i == TILES - 1), skip_group_check=True)
                last.then_inc(seg_done, 1)

            first(0, 0, 16, False)
            first(1, 1, 16, False)
            second(0, 0, False)
            for c in range(BODY):
                first(c + 2, c + 2, 16 * ((c + 2) // BODY + 1))
                second(c + 1, c + 1)
                segment(c, c, c >= 2)
            with pe.Fori(1, CHUNKS // BODY - 1) as j:
                for s in range(BODY):
                    first(j * BODY + (s + 2), s + 2, j * 16 + 16 * ((s + 2) // BODY + 1))
                    second(j * BODY + (s + 1), s + 1)
                    segment(j * BODY + s, s)
            for c in range(CHUNKS - BODY, CHUNKS):
                if c + 2 < CHUNKS:
                    first(c + 2, c + 2, 16 * ((c + 2) // BODY + 1))
                if c + 1 < CHUNKS:
                    second(c + 1, c + 1)
                segment(c, c)
            pe.wait_ge(sums_added, 2 * CHUNKS)
            for f in range(FINALS):
                if f >= 2:
                    pe.wait_ge(y_ready, f - 1)
                for b in range(FINAL):
                    n = f * FINAL + b
                    last = pe.matmul(p_seg[f % 2][:, b * D:(b + 1) * D], sums[:, n * P:(n + 1) * P], fold[:, :],
                                     start=True, stop=True, skip_group_check=True)
                last.then_inc(fold_done, 1)


def kernel(x, src, dst, edge_attr_64, L0_gnn_W1, L0_gnn_b1, L0_gnn_W2, L0_gnn_b2,
           L0_gnn_G1, L0_gnn_g1, L0_gnn_G2, L0_gnn_g2):
    import concourse.bacc as bacc
    from concourse.bass_utils import run_bass_kernel_spmd

    f32 = np.float32
    e = np.zeros((CHUNKS * CHUNK, D), f32)
    e[:EDGES] = np.asarray(edge_attr_64)
    d = np.full((CHUNKS * CHUNK,), NODES, np.int32)
    d[:EDGES] = np.asarray(dst)
    n = np.zeros((NODES_PAD, D), f32)
    n[:NODES] = np.asarray(x)
    w1g1 = np.concatenate([np.asarray(L0_gnn_W1), np.asarray(L0_gnn_G1)], 1)
    arrays = {
        "x_nodes": n.reshape(BLOCKS, P, D).transpose(1, 0, 2),
        "x_edges": e.reshape(CHUNKS, 2, HALF, D).transpose(1, 3, 0, 2).reshape(P, CHUNKS, HALF),
        "dst_halves": d.reshape(HALF_ROWS, HALF_COLS, HALF),
        "dst_tiles": d.reshape(HALVES, TILES, TILE).transpose(2, 0, 1),
        "w_first": w1g1,
        "w_second": np.concatenate([np.asarray(L0_gnn_W2), np.asarray(L0_gnn_G2)], 0),
        "b_first": np.concatenate([np.asarray(L0_gnn_b1), np.asarray(L0_gnn_g1)]).reshape(P, 1),
        "b_second": np.concatenate([np.asarray(L0_gnn_b2), np.asarray(L0_gnn_g2)]).reshape(1, P),
    }
    arrays = {k: np.ascontiguousarray(v) for k, v in arrays.items()}
    nc = bacc.Bacc("TRN2", target_bir_lowering=False, num_devices=1)
    args = [nc.dram_tensor(k, v.shape, mybir.dt.from_np(v.dtype), kind="ExternalInput").ap()
            for k, v in arrays.items()]
    out = nc.dram_tensor("out", (P, BLOCKS, D), mybir.dt.float32, kind="ExternalOutput").ap()
    build(nc, *args, out)
    r = run_bass_kernel_spmd(nc, [arrays], core_ids=[0])
    return np.ascontiguousarray(r.results[0]["out"].transpose(1, 0, 2).reshape(NODES_PAD, D)[:NODES])
```

```python
import numpy as np

import concourse.bass as bass
from concourse import mybir
from contextlib import ExitStack

P = 128
D = 64
NODES = 12500
EDGES = 400000
TILE = 128
TILES = 4
HALF = TILE * TILES
CHUNK = 2 * HALF
BODY = 4
CHUNKS = -(-EDGES // (CHUNK * BODY)) * BODY
HALVES = 2 * CHUNKS
HALF_ROWS = 112
HALF_COLS = HALVES // HALF_ROWS
DST_PARTS = slice(0, HALF_COLS // 2), slice(HALF_COLS // 2, HALF_COLS)
WINDOW = 48
BLOCKS = -(-NODES // P)
NODES_PAD = BLOCKS * P
SUM_COLS = -(-NODES_PAD // WINDOW) * WINDOW
HEAD = 2 * BODY
LEAD = 3
SLOTS = 4
NODE_LOADS = 7
SCALE = D // 2
ZEROS = SUM_COLS // 4, SUM_COLS * 3 // 4
WINDOWS = SUM_COLS // WINDOW
LAST_BASE = SUM_COLS - WINDOW
FINAL = 7
FINALS = BLOCKS // FINAL
FOLD = D + D // 2
EPS = 1e-5
assert (FINAL + 1) * D <= HALF
assert HALF_ROWS * HALF_COLS == HALVES and FINALS * FINAL == BLOCKS and CHUNKS % BODY == 0
assert BLOCKS == CHUNKS // BODY


def build(nc, x_nodes, x_edges, dst_halves, dst_tiles, first_weights, second_weights, b_first, b_second, out):
    fp32, fp32r, bf16, i32 = mybir.dt.float32, mybir.dt.float32r, mybir.dt.bfloat16, mybir.dt.int32
    ALU, ACT, AX = mybir.AluOpType, mybir.ActivationFunctionType, mybir.AxisListType

    def exists(c):
        return not isinstance(c, int) or 0 <= c < CHUNKS

    def wait(eng, sem, value):
        if not isinstance(value, int) or value > 0:
            eng.wait_ge(sem, value)

    def pipeline(eng, step):
        for s in range(-LEAD, BODY):
            step(0, s)
        with eng.Fori(1, CHUNKS // BODY - 1) as j:
            for s in range(BODY):
                step(j, s)
        for s in range(BODY + LEAD):
            step(CHUNKS // BODY - 1, s)

    with ExitStack() as ctx:
        def sb(name, shape, dt=fp32):
            return ctx.enter_context(nc.sbuf_tensor(name, shape, dt))

        def ps(name, shape):
            return ctx.enter_context(nc.psum_tensor(name, shape, fp32))

        def sem(name):
            return ctx.enter_context(nc.semaphore(name))

        w1g1 = sb("w1g1", [P, P])
        w1g1_high = sb("w1g1_high", [P, P], fp32r)
        w1g1_low = sb("w1g1_low", [P, P], fp32r)
        w2g2 = sb("w2g2", [P, P])
        b1g1 = sb("b1g1", [P, 1])
        bias_in = sb("bias_in", [P, P])
        bias_rest = sb("bias_rest", [P, 2, P])
        bias_rows = sb("bias_rows", [P, P], bf16)
        bias_ones = sb("bias_ones", [P, P], bf16)
        iota = sb("iota", [P, WINDOW])
        fold = sb("fold", [P, FOLD])
        x_in = [sb(f"x_in{s}", [P, HALF]) for s in range(SLOTS)]
        x_parts = [sb(f"x_parts{s}", [P, 2, HALF], fp32r) for s in range(2)]
        hidden = [sb(f"hidden{s}", [P, 2, HALF]) for s in range(2)]
        silu = [sb(f"silu{s}", [P, 2 * TILES, D]) for s in range(2)]
        gate = [sb(f"gate{s}", [P, 2 * TILES, D]) for s in range(2)]
        msg = [sb(f"msg{s}", [P, 2 * TILES, 2, D]) for s in range(2)]
        msg_low = [sb(f"msg_low{s}", [P, 2 * TILES, 2, D], bf16) for s in range(2)]
        onehot = [sb(f"onehot{s}", [P, 2 * TILES, WINDOW], bf16) for s in range(2)]
        dst_head = sb("dst_head", [HEAD, HALF], i32)
        head_least = sb("head_least", [HEAD, 2])
        head_base = sb("head_base", [HEAD, 1], i32)
        dst_h = sb("dst_h", [HALF_ROWS, HALF_COLS, HALF], i32)
        ends = sb("ends", [HALF_ROWS, 3, HALF_COLS])
        base_span = sb("base_span", [HALF_ROWS, 2, HALF_COLS], i32)
        dst_t = sb("dst_t", [P, HALVES, TILES], i32)
        base = sb("base", [P, HALVES], i32)
        row_span = sb("row_span", [HALF_ROWS, 1], i32)
        row_spans = sb("row_spans", [1, HALF_ROWS], i32)
        span = sb("span", [1, HALVES], i32)
        chunk_span = sb("chunk_span", [1, CHUNKS], i32)
        most_span = sb("most_span", [1, 1], i32)
        rel = sb("rel", [P, HALVES, TILES])
        target = sb("target", [P, 2, TILES])
        sums = sb("sums", [P, SUM_COLS])
        x_n = sb("x_n", [P, BLOCKS, D])
        x_sum = sb("x_sum", [P, BLOCKS])
        sq = [sb(f"sq{s}", [P, FINAL, D]) for s in range(2)]
        stat = sb("stat", [P, 4, BLOCKS])
        warm = sb("warm", [1, 1])

        p_first = [ps(f"p_first{s}", [P, 2, HALF]) for s in range(2)]
        p_second = ps("p_second", [P, 2 * TILES, 2, D])
        p_seg = [ps(f"p_seg{s}", [P, 512]) for s in range(2)]

        scratch = nc.dram_tensor("base_span_scratch", (2, HALF_ROWS, HALF_COLS), i32, kind="Internal").ap()

        row_scratch = nc.dram_tensor("row_span_scratch", (HALF_ROWS, 1), i32, kind="Internal").ap()
        head_scratch = nc.dram_tensor("head_scratch", (HEAD, 1), i32, kind="Internal").ap()

        w1_in, w2_in, b1_in, b2_in = sem("w1_in"), sem("w2_in"), sem("b1_in"), sem("b2_in")
        x_loaded = [sem(f"x_loaded{s}") for s in range(SLOTS)]
        dst_h_in, dst_t_in = [sem(f"dst_h_in{k}") for k in range(2)], [sem(f"dst_t_in{k}") for k in range(2)]
        base_out, base_in = sem("base_out"), sem("base_in")
        head_in, head_step, head_ready = sem("head_in"), sem("head_step"), sem("head_ready")
        row_ready, row_out, row_in = sem("row_ready"), sem("row_out"), sem("row_in")
        head_out, head_base_in = sem("head_out"), sem("head_base_in")
        span_ready, span_out, span_in = sem("span_ready"), sem("span_out"), sem("span_in")
        x_n_in, x_summed, x_centred = sem("x_n_in"), sem("x_summed"), sem("x_centred")
        consts, weights_split = sem("consts"), sem("weights_split")
        bias_ones_ready, bias_step = sem("bias_ones_ready"), sem("bias_step")
        msg_low_zero, sums_zero = sem("msg_low_zero"), sem("sums_zero")
        ends_step, base_ready, rel_ready = sem("ends_step"), sem("base_ready"), sem("rel_ready")
        greatest, most_ready, chunk_span_ready = sem("greatest"), sem("most_ready"), sem("chunk_span_ready")
        high_ready, parts_ready = sem("high_ready"), sem("parts_ready")
        first_done, hidden_ready = sem("first_done"), sem("hidden_ready")
        second_done, silu_ready, gate_ready = sem("second_done"), sem("silu_ready"), sem("gate_ready")
        onehot_ready, msg_ready = sem("onehot_ready"), sem("msg_ready")
        rest_ready, low_ready = sem("rest_ready"), sem("low_ready")
        seg_done, sums_added = sem("seg_done"), sem("sums_added")
        w_x, w_high, w_parts, w_first = sem("sweep_x"), sem("sweep_high"), sem("sweep_parts"), sem("sweep_first")
        w_hidden, w_second, w_silu, w_gate = sem("sweep_hidden"), sem("sweep_second"), sem("sweep_silu"), sem("sweep_gate")
        w_msg, w_rest, w_low = sem("sweep_msg"), sem("sweep_rest"), sem("sweep_low")
        w_target, w_onehot, w_seg, w_added = sem("sweep_target"), sem("sweep_onehot"), sem("sweep_seg"), sem("sweep_added")
        swept = sem("swept")
        fold_done, y_ready = sem("fold_done"), sem("y_ready")
        squared, summed, var_ready, std_ready = sem("squared"), sem("summed"), sem("var_ready"), sem("std_ready")
        rstd_ready, normed, last_normed = sem("rstd_ready"), sem("normed"), sem("last_normed")
        stored = sem("stored")

        def folded(f):
            return p_first[f // 2 % 2][:, f % 2, :]

        def sweep(eng, chunk_work, sems, before=None, after=None, settle=None):
            eng.wait_ge(most_ready, 1)
            most = eng.value_load(most_span[0:1, 0:1])
            with eng.If(most > WINDOW - 1):
                if before:
                    before()
                eng.wait_ge(chunk_span_ready, 1)
                with eng.Fori(0, CHUNKS) as c:
                    wide = eng.value_load(chunk_span[0:1, bass.ds(c, 1)])
                    with eng.If(wide > WINDOW - 1):
                        chunk_work(c)
                    with eng.Else():
                        settle(c) if settle else eng.drain()
                        for sem, by in sems:
                            eng.sem_inc(sem, by)
                if after:
                    after()

        def norm(eng, f, normed):
            cols = slice(f * FINAL, (f + 1) * FINAL)
            eng.wait_ge(rstd_ready, f + 1)
            eng.tensor_tensor(x_n[:, cols, :], x_n[:, cols, :],
                              stat[:, 3, cols].rearrange("p (b o) -> p b o", o=1).broadcast_to([P, FINAL, D]),
                              ALU.mult).then_inc(normed, 1)

        block = ctx.enter_context(nc.Block())

        @block.sync
        def _(sp):
            def load_x(j, s):
                sp.dma_start(x_in[s][:, :], x_edges[:, bass.ds(j * SLOTS + s, 1), :].rearrange("p a n -> p (a n)"))\
                  .then_inc(x_loaded[s], 16)

            def load_dst_h(k):
                part = DST_PARTS[k]
                sp.dma_start(dst_h[:, part, :], dst_halves[:, part, :]).then_inc(dst_h_in[k], 16)

            def load_dst_t(k):
                part = slice(0, HEAD) if k == 0 else slice(HEAD, HALVES)
                sp.dma_start(dst_t[:, part, :], dst_tiles[:, part, :]).then_inc(dst_t_in[k], 16)

            def load_nodes(n):
                part = slice(BLOCKS * n // NODE_LOADS, BLOCKS * (n + 1) // NODE_LOADS)
                sp.dma_start(x_n[:, part, :], x_nodes[:, part, :]).then_inc(x_n_in, 16)

            load_x(0, 0)
            load_x(0, 1)
            sp.dma_start(dst_head[:, :], dst_halves.rearrange("r c n -> (r c) n")[0:HEAD]).then_inc(head_in, 16)
            sp.dma_start(b1g1[:, :], b_first).then_inc(b1_in, 16)
            load_dst_h(0)
            load_x(0, 2)
            load_x(0, 3)
            load_dst_h(1)
            load_dst_t(0)
            sp.wait_ge(head_ready, 1)
            sp.dma_start(head_scratch, head_base[:, :]).then_inc(head_out, 16)
            sp.wait_ge(parts_ready, 2)
            load_x(1, 0)
            sp.wait_ge(head_out, 16)
            sp.dma_start(base[:, 0:HEAD], head_scratch.rearrange("h o -> (h o)").partition_broadcast(P))\
              .then_inc(head_base_in, 16)
            sp.wait_ge(parts_ready, 4)
            load_x(1, 1)
            sp.wait_ge(base_ready, 1)
            sp.dma_start(scratch[0], base_span[:, 0, :]).then_inc(base_out, 16)
            sp.wait_ge(parts_ready, 6)
            load_x(1, 2)
            sp.wait_ge(base_out, 16)
            sp.dma_start(base[:, HEAD:], scratch[0].rearrange("r h -> (r h)")[HEAD:].partition_broadcast(P))\
              .then_inc(base_in, 16)
            sp.wait_ge(parts_ready, 8)
            load_x(1, 3)
            load_dst_t(1)
            for s in range(SLOTS):
                sp.wait_ge(parts_ready, (s + 1 + SLOTS) * 2)
                load_x(2, s)
                for n in range(NODE_LOADS * s // SLOTS, NODE_LOADS * (s + 1) // SLOTS):
                    load_nodes(n)
            with sp.Fori(3, CHUNKS // SLOTS) as j:
                for s in range(SLOTS):
                    sp.wait_ge(parts_ready, (j * SLOTS + (s + 1 - SLOTS)) * 2)
                    load_x(j, s)

            def chunk_work(c):
                sp.wait_ge(w_added, c * WINDOWS + 1)
                sp.dma_start(x_in[0][:, :], x_edges[:, bass.ds(c, 1), :].rearrange("p a n -> p (a n)"))\
                  .then_inc(w_x, 16)

            def before():
                sp.wait_ge(sums_added, HALVES)
                sp.sem_inc(w_x, 16)

            sp.wait_ge(span_ready, 1)
            sp.dma_start(scratch[1], base_span[:, 1, :]).then_inc(span_out, 16)
            sp.wait_ge(row_ready, 1)
            sp.dma_start(row_scratch, row_span[:, :]).then_inc(row_out, 16)
            sp.wait_ge(row_out, 16)
            sp.dma_start(row_spans[:, :], row_scratch.rearrange("r o -> o r")).then_inc(row_in, 16)
            sp.wait_ge(span_out, 16)
            sp.dma_start(span[:, :], scratch[1:2].rearrange("k r h -> k (r h)")).then_inc(span_in, 16)
            sweep(sp, chunk_work, [(w_x, 16)], before, settle=lambda c: sp.wait_ge(w_x, c * 16 + 16))
            for f in range(FINALS):
                if f < FINALS - 1:
                    sp.wait_ge(normed, f + 1)
                else:
                    sp.wait_ge(last_normed, 1)
                sp.dma_start(out[:, f * FINAL:(f + 1) * FINAL, :], x_n[:, f * FINAL:(f + 1) * FINAL, :])\
                  .then_inc(stored, 16)
            sp.wait_ge(span_in, 16)
            sp.wait_ge(stored, 16 * FINALS)

        @block.gpsimd
        def _(pool):
            pool.memset(bias_ones[:, :], 0.0).then_inc(bias_ones_ready, 1)
            for k in range(3):
                pool.wait_ge(bias_ones_ready, k + 1)
                pool.memset(bias_ones[32 * k:32 * k + 1, :], 1.0).then_inc(bias_ones_ready, 1)
            pool.wait_ge(bias_ones_ready, 4)
            for s in range(2):
                pool.memset(msg_low[s][:, :, 1, :], 0.0).then_inc(msg_low_zero, 1)
            pool.memset(sums[:, 0:ZEROS[0]], 0.0).then_inc(sums_zero, 1)
            pool.wait_ge(b2_in, 16)
            pool.wait_ge(msg_low_zero, 2)
            pool.tensor_copy(bias_rows[:, :], bias_in[:, :]).then_inc(bias_step, 1)
            pool.wait_ge(bias_step, 1)
            pool.tensor_tensor(bias_rest[:, 0, :], bias_in[:, :], bias_rows[:, :], ALU.subtract).then_inc(bias_step, 1)
            pool.wait_ge(bias_step, 2)
            for k, rows in enumerate((slice(32, 64), slice(64, P))):
                pool.tensor_copy(bias_rows[rows, :], bias_rest[rows, 0, :]).then_inc(bias_step, 1)
                pool.wait_ge(bias_step, 3 + k)
            pool.tensor_tensor(bias_rest[64:P, 1, :], bias_rest[64:P, 0, :], bias_rows[64:P, :], ALU.subtract)\
                .then_inc(bias_step, 1)
            pool.wait_ge(bias_step, 5)
            pool.tensor_copy(bias_rows[64:P, :], bias_rest[64:P, 1, :]).then_inc(bias_step, 1)
            pool.wait_ge(bias_step, 6)
            pool.iota(iota[:, :], [[1, WINDOW]], base=0, channel_multiplier=0,
                      allow_small_or_imprecise_dtypes=True).then_inc(consts, 1)
            pool.memset(fold[:, 0:D], -SCALE / 2 / D).then_inc(consts, 1)
            pool.memset(fold[:, D:], 0.0).then_inc(consts, 1)
            pool.wait_ge(consts, 3)
            for h in range(2):
                pool.affine_select(out=fold[:, 0:D], in_=fold[:, 0:D], compare_op=ALU.not_equal, fill=SCALE / 2 * (1 - 1 / D),
                                   base=-D * h, pattern=[[-1, D]], channel_multiplier=1).then_inc(consts, 1)
                pool.wait_ge(consts, 4 + h)
            pool.memset(sums[:, ZEROS[0]:ZEROS[1]], 0.0).then_inc(sums_zero, 1)

            def upper(ap):
                return ap.bitcast(bf16).rearrange("p t (d two) -> p t d two", two=2)[:, :, :, 1]

            def split(c, s, msg_ready, rest_ready, low_ready):
                pool.wait_ge(msg_ready, c + 1)
                whole, rest = msg[s % 2][:, :, 0, :], msg[s % 2][:, :, 1, :]
                pool.tensor_tensor(rest, whole, upper(whole), ALU.subtract).then_inc(rest_ready, 1)
                pool.wait_ge(rest_ready, c + 1)
                pool.tensor_tensor(msg_low[s % 2][:, :, 0, :], rest, upper(rest), ALU.subtract)\
                    .then_inc(low_ready, 1)

            for s in range(BODY):
                split(s, s, msg_ready, rest_ready, low_ready)
                if s == 0:
                    pool.memset(sums[:, ZEROS[1]:], 0.0).then_inc(sums_zero, 1)
            with pool.Fori(1, CHUNKS // BODY) as j:
                for s in range(BODY):
                    split(j * BODY + s, s, msg_ready, rest_ready, low_ready)
            sweep(pool, lambda c: split(c, 0, w_msg, w_rest, w_low), [(w_rest, 1), (w_low, 1)])
            for f in range(FINALS - 1):
                norm(pool, f, normed)

        @block.scalar
        def _(act):
            act.dma_start(w1g1[:, :], first_weights).then_inc(w1_in, 16)
            act.dma_start(bias_in[:, :], b_second.rearrange("o n -> (o n)").partition_broadcast(P)).then_inc(b2_in, 16)
            act.wait_ge(bias_ones_ready, 4)
            act.activation(warm[:, :], bias_ones[0:1, 0:1], ACT.Silu)
            act.dma_start(w2g2[:, :], second_weights).then_inc(w2_in, 16)

            def high(s, high_ready):
                for h in range(2):
                    rows = slice(D * h, D * h + D)
                    act.activation(x_parts[s % 2][rows, h, :], x_in[s % SLOTS][rows, :], ACT.Copy)\
                       .then_inc(high_ready, 1)

            def first(s, hidden_ready):
                act.activation(hidden[s % 2][:, :, :], p_first[s % 2][:, :, :], ACT.Silu, bias=b1g1[:, 0:1])\
                   .then_inc(hidden_ready, 1)

            def second(s, silu_ready, gate_ready):
                act.activation(silu[s % 2][:, :, :], p_second[:, :, 0, :], ACT.Silu).then_inc(silu_ready, 1)
                act.activation(gate[s % 2][:, :, :], p_second[:, :, 1, :], ACT.Tanh, scale=0.5).then_inc(gate_ready, 1)

            def step(j, s):
                c = j * BODY + s
                if exists(c + 1):
                    if isinstance(j, int) and c == -1:
                        act.wait_ge(b1_in, 16)
                    wait(act, first_done, c + 2)
                    wait(act, second_done, c)
                    first(s + 1, hidden_ready)
                if exists(c + 3):
                    act.wait_ge(x_loaded[(s + 3) % SLOTS], j * 16 + 16 * ((s + 3) // SLOTS + 1))
                    wait(act, first_done, c + 2)
                    high(s + 3, high_ready)
                if exists(c):
                    act.wait_ge(second_done, c + 1)
                    wait(act, msg_ready, c - 1)
                    second(s, silu_ready, gate_ready)

            pipeline(act, step)

            def chunk_work(c):
                act.wait_ge(w_x, c * 16 + 32)
                high(0, w_high)
                act.wait_ge(w_first, c + 1)
                first(0, w_hidden)
                act.wait_ge(w_second, c + 1)
                second(0, w_silu, w_gate)

            sweep(act, chunk_work, [(w_high, 2), (w_hidden, 1), (w_silu, 1), (w_gate, 1)])
            for f in range(FINALS + 1):
                if f < FINALS:
                    act.wait_ge(y_ready, f + 1)
                    if f >= 2:
                        act.wait_ge(summed, f - 1)
                    act.activation(sq[f % 2][:, :, :], x_n[:, f * FINAL:(f + 1) * FINAL, :], ACT.Square)\
                       .then_inc(squared, 1)
                if f:
                    cols = slice((f - 1) * FINAL, f * FINAL)
                    act.wait_ge(var_ready, f)
                    act.activation(stat[:, 2, cols], stat[:, 1, cols], ACT.Sqrt).then_inc(std_ready, 1)

        @block.vector
        def _(dve):
            dve.wait_ge(w1_in, 16)
            dve.tensor_copy(w1g1_high[:, :], w1g1[:, :]).then_inc(weights_split, 1)
            dve.wait_ge(weights_split, 1)
            dve.tensor_tensor(w1g1_low[:, :], w1g1[:, :], w1g1_high[:, :].bitcast(fp32), ALU.subtract)\
               .then_inc(weights_split, 1)

            def low(s, parts_ready):
                for h in range(2):
                    rows, other = slice(D * h, D * h + D), slice(D - D * h, 2 * D - D * h)
                    dve.tensor_tensor(x_parts[s % 2][other, h, :], x_in[s % SLOTS][rows, :],
                                      x_parts[s % 2][rows, h, :].bitcast(fp32), ALU.subtract)\
                       .then_inc(parts_ready, 1)

            def hot(s, relative, onehot_ready):
                dve.tensor_tensor(onehot[s % 2][:, :, :],
                                  iota[:, :].rearrange("p (o w) -> p o w", o=1).broadcast_to([P, 2 * TILES, WINDOW]),
                                  relative.rearrange("p h (i o) -> p (h i) o", o=1)
                                  .broadcast_to([P, 2 * TILES, WINDOW]),
                                  ALU.is_equal).then_inc(onehot_ready, 1)

            def message(s, msg_ready):
                dve.scalar_tensor_tensor(msg[s % 2][:, :, 0, :], gate[s % 2][:, :, :], 1.0, silu[s % 2][:, :, :],
                                         ALU.add, ALU.mult).then_inc(msg_ready, 1)

            def window_starts(c):
                return [dve.value_load(base[0:1, bass.ds(c * 2 + h, 1)], min_val=0, max_val=LAST_BASE)
                        for h in range(2)]

            def gated(c, s):
                dve.wait_ge(silu_ready, c + 1)
                dve.wait_ge(gate_ready, c + 1)
                message(s, msg_ready)

            def step(j, s):
                c = j * BODY + s
                if exists(c + 3):
                    dve.wait_ge(high_ready, (c + 4) * 2)
                    wait(dve, first_done, c + 2)
                    low(s + 3, parts_ready)
                if isinstance(j, int) and c == -2:
                    head_windows()
                    windows(0)
                if isinstance(j, int) and c == 0:
                    gated(c, s)
                    windows(1)
                    dve.wait_ge(dst_t_in[0], 16)
                    dve.wait_ge(head_base_in, 16)
                    relative(0)
                    dve.wait_ge(consts, 5)
                if exists(c) and s == 0:
                    dve.wait_ge(rel_ready, j + 1)
                if isinstance(j, int) and c == CHUNKS - 1:
                    starts = window_starts(c - 2)
                if exists(c):
                    wait(dve, seg_done, c - 1)
                    hot(s, rel[:, bass.ds(c * 2, 2), :], onehot_ready)
                if exists(c) and not (isinstance(j, int) and c == 0):
                    gated(c, s)
                if isinstance(j, int) and c == CHUNKS - 1:
                    most()
                if isinstance(j, int) and c == 2:
                    dve.wait_ge(sums_zero, 3)
                if exists(c - 2):
                    if not (isinstance(j, int) and c == CHUNKS - 1):
                        starts = window_starts(c - 2)
                    dve.wait_ge(seg_done, c - 1)
                    for h in range(2):
                        wait(dve, sums_added, c * 2 + (h - 4))
                        dve.tensor_tensor(sums[:, bass.ds(starts[h], WINDOW)], sums[:, bass.ds(starts[h], WINDOW)],
                                          p_seg[s % 2][:, h * WINDOW:(h + 1) * WINDOW], ALU.add)\
                           .then_inc(sums_added, 1)
                if isinstance(j, int):
                    for k, at in enumerate((3, CHUNKS - BODY, CHUNKS - BODY + 1)):
                        if c == at:
                            spans(k)
                if s == 3 and exists(c) and exists(c + BODY):
                    if isinstance(j, int) and j == 0:
                        dve.wait_ge(dst_t_in[1], 16)
                        dve.wait_ge(base_in, 16)
                    relative(j + 1)
                if not isinstance(j, int) or j > 0:
                    if s == 2:
                        centre_sum(j)
                    if s == 3:
                        centre(j)
                    if isinstance(j, int) and c == CHUNKS:
                        centre_sum(j + 1)
                    if isinstance(j, int) and c == CHUNKS + 1:
                        centre(j + 1)

            def relative(j):
                halves = bass.ds(j * (2 * BODY), 2 * BODY)
                dve.tensor_tensor(rel[:, halves, :], dst_t[:, halves, :],
                                  base[:, halves].rearrange("p (h o) -> p h o", o=1).broadcast_to([P, 2 * BODY, TILES]),
                                  ALU.subtract).then_inc(rel_ready, 1)

            def centre_sum(j):
                dve.wait_ge(x_n_in, 16 * NODE_LOADS)
                b = bass.ds(j - 1, 1)
                dve.tensor_reduce(x_sum[:, b], x_n[:, b, :], AX.X, ALU.add).then_inc(x_summed, 1)

            def centre(j):
                dve.wait_ge(x_summed, j)
                b = bass.ds(j - 1, 1)
                x_b = x_n[:, b, :].rearrange("p a d -> p (a d)")
                dve.tensor_scalar(x_b, x_b, float(D), x_sum[:, b], ALU.mult, ALU.subtract).then_inc(x_centred, 1)

            def head_windows():
                dve.wait_ge(head_in, 16)
                dve.tensor_reduce(head_least[:, 0:1], dst_head[:, :], AX.X, ALU.min).then_inc(head_step, 1)
                dve.wait_ge(head_step, 1)
                dve.tensor_scalar(head_least[:, 1:2], head_least[:, 0:1], 0.0, float(LAST_BASE), ALU.max, ALU.min)\
                   .then_inc(head_step, 1)
                dve.wait_ge(head_step, 2)
                dve.tensor_copy(head_base[:, :], head_least[:, 1:2]).then_inc(head_ready, 1)

            def windows(k):
                part = DST_PARTS[k]
                dve.wait_ge(dst_h_in[k], 16)
                dve.tensor_reduce(ends[:, 0, part], dst_h[:, part, :], AX.X, ALU.min).then_inc(ends_step, 1)
                if k == 0:
                    return
                dve.wait_ge(ends_step, 2)
                dve.tensor_scalar(ends[:, 2, :], ends[:, 0, :], 0.0, float(LAST_BASE), ALU.max, ALU.min)\
                   .then_inc(ends_step, 1)
                dve.wait_ge(ends_step, 3)
                dve.tensor_copy(base_span[:, 0, :], ends[:, 2, :]).then_inc(base_ready, 1)

            def spans(k):
                part = slice(-(-HALF_COLS * k // 3), -(-HALF_COLS * (k + 1) // 3))
                dve.tensor_reduce(ends[:, 1, part], dst_h[:, part, :], AX.X, ALU.max).then_inc(greatest, 1)
                if k == 2:
                    dve.wait_ge(greatest, 3)
                    dve.tensor_tensor(base_span[:, 1, :], ends[:, 1, :], ends[:, 2, :], ALU.subtract)\
                       .then_inc(span_ready, 1)
                    dve.wait_ge(span_ready, 1)
                    dve.tensor_reduce(row_span[:, :], base_span[:, 1, :], AX.X, ALU.max).then_inc(row_ready, 1)

            def most():
                dve.wait_ge(row_in, 16)
                dve.tensor_reduce(most_span[:, :], row_spans[:, :], AX.X, ALU.max).then_inc(most_ready, 1)

            pipeline(dve, step)

            def chunk_work(c):
                dve.wait_ge(w_high, c * 2 + 2)
                low(0, w_parts)
                halves = bass.ds(c * 2, 2)
                dve.tensor_scalar(target[:, :, :], rel[:, halves, :], float(WINDOW), float(1 << 20),
                                  ALU.is_lt, ALU.mult).then_inc(w_target, 1)
                dve.wait_ge(w_target, c * (2 + WINDOWS) + 1)
                dve.tensor_tensor(target[:, :, :], target[:, :, :], dst_t[:, halves, :], ALU.add).then_inc(w_target, 1)
                dve.wait_ge(w_silu, c + 1)
                dve.wait_ge(w_gate, c + 1)
                message(0, w_msg)
                with dve.Fori(0, WINDOWS) as w:
                    n = c * WINDOWS + w
                    dve.wait_ge(w_target, c * (2 + WINDOWS) + w + 2)
                    hot(0, target[:, :, :], w_onehot)
                    dve.wait_ge(w_onehot, n + 1)
                    dve.tensor_scalar(target[:, :, :], target[:, :, :], float(WINDOW), None, ALU.subtract)\
                       .then_inc(w_target, 1)
                    dve.wait_ge(w_seg, n + 1)
                    window = bass.ds(w * WINDOW, WINDOW)
                    dve.tensor_tensor(sums[:, window], sums[:, window], p_seg[0][:, 0:WINDOW], ALU.add)\
                       .then_inc(w_added, 1)

            def before():
                dve.wait_ge(span_in, 16)
                dve.tensor_reduce(chunk_span[:, :], span[:, :].rearrange("p (c h) -> p c h", h=2), AX.X, ALU.max)\
                   .then_inc(chunk_span_ready, 1)
                dve.wait_ge(sums_added, HALVES)
                dve.sem_inc(w_added, 1)

            sweep(dve, chunk_work, [(w_parts, 2), (w_target, 2 + WINDOWS), (w_msg, 1), (w_onehot, WINDOWS),
                                    (w_added, WINDOWS)], before,
                  after=lambda: dve.drain().then_inc(swept, 1))

            def residual(f):
                cols = slice(f * FINAL, (f + 1) * FINAL)
                dve.wait_ge(fold_done, f + 1)
                if f == 0:
                    dve.wait_ge(x_centred, BLOCKS)
                x_f = x_n[:, cols, :].rearrange("p b d -> p (b d)")
                dve.tensor_tensor(x_f, x_f, folded(f)[:, 0:FINAL * D], ALU.add).then_inc(y_ready, 1)

            def variance(f):
                cols = slice(f * FINAL, (f + 1) * FINAL)
                dve.wait_ge(squared, f + 1)
                dve.tensor_reduce(stat[:, 0, cols], sq[f % 2][:, :, :], AX.X, ALU.add).then_inc(summed, 1)
                dve.wait_ge(summed, f + 1)
                dve.tensor_scalar(stat[:, 1, cols], stat[:, 0, cols], 1.0 / D, EPS * SCALE * SCALE, ALU.mult, ALU.add)\
                   .then_inc(var_ready, 1)

            def inverse(f):
                cols = slice(f * FINAL, (f + 1) * FINAL)
                dve.wait_ge(std_ready, f + 1)
                dve.reciprocal(stat[:, 3, cols], stat[:, 2, cols]).then_inc(rstd_ready, 1)

            for f in range(FINALS + 2):
                if f < FINALS:
                    residual(f)
                if 0 < f <= FINALS:
                    variance(f - 1)
                if f > 1:
                    inverse(f - 2)
            norm(dve, FINALS - 1, last_normed)

        @block.tensor
        def _(pe):
            def keep_warm(n):
                for _ in range(n):
                    pe.matmul(p_first[0][:, 0, :], bias_ones[:, :],
                              bias_ones[:, :].rearrange("p (o n) -> p o n", o=1).broadcast_to([P, TILES, P]),
                              start=True, stop=True, skip_group_check=True)

            pe.wait_ge(bias_ones_ready, 4)
            keep_warm(11)
            pe.wait_ge(weights_split, 2)

            def first(s, first_done):
                for h in range(2):
                    for k, w in enumerate((w1g1_high, w1g1_low)):
                        last = pe.matmul(p_first[s % 2][:, h, :], w[:, :], x_parts[s % 2][:, h, :],
                                         start=(k == 0), stop=(k == 1))
                last.then_inc(first_done, 1)

            def second(s, second_done):
                for h in range(2):
                    pe.matmul(p_second[:, h * TILES:(h + 1) * TILES, :, :], bias_ones[:, :],
                              bias_rows[:, :].rearrange("p (o n) -> p o n", o=1).broadcast_to([P, TILES, P]),
                              start=True, stop=False, skip_group_check=True)
                for t in range(2 * TILES):
                    h, i = divmod(t, TILES)
                    last = pe.matmul(p_second[:, t, :, :], hidden[s % 2][:, h, i * TILE:(i + 1) * TILE],
                                     w2g2[:, :], start=False, stop=True, skip_group_check=True)
                last.then_inc(second_done, 1)

            def segment(s, windows, seg_done):
                for t in range(2 * TILES):
                    n = t // TILES if windows == 2 else 0
                    window = p_seg[s % 2][:, n * WINDOW:(n + 1) * WINDOW]
                    tiles = 2 * TILES // windows
                    parts = msg[s % 2][:, t, :, :].rearrange("p k d -> p (k d)").bitcast(bf16)\
                        .rearrange("p (d two) -> p d two", two=2)[:, :, 1]
                    pe.matmul(window, parts, onehot[s % 2][:, t, :], start=(t % tiles == 0), stop=False,
                              skip_group_check=True)
                    last = pe.matmul(window, msg_low[s % 2][:, t, :, :], onehot[s % 2][:, t, :],
                                     start=False, stop=(t % tiles == tiles - 1), skip_group_check=True)
                last.then_inc(seg_done, 1)

            def step(j, s):
                c = j * BODY + s
                if exists(c + 2):
                    pe.wait_ge(parts_ready, (c + 3) * 2)
                    wait(pe, hidden_ready, c + 1)
                    first(s + 2, first_done)
                if exists(c + 1):
                    if isinstance(j, int) and c == -1:
                        pe.wait_ge(bias_step, 6)
                        pe.wait_ge(w2_in, 16)
                    pe.wait_ge(hidden_ready, c + 2)
                    wait(pe, silu_ready, c + 1)
                    wait(pe, gate_ready, c + 1)
                    second(s + 1, second_done)
                if exists(c - 1):
                    if isinstance(j, int) and c == CHUNKS:
                        keep_warm(10)
                    pe.wait_ge(onehot_ready, c)
                    pe.wait_ge(low_ready, c)
                    wait(pe, sums_added, c * 2 - 4)
                    segment(s - 1, 2, seg_done)

            pipeline(pe, step)

            def chunk_work(c):
                pe.wait_ge(w_parts, c * 2 + 2)
                first(0, w_first)
                pe.wait_ge(w_hidden, c + 1)
                second(0, w_second)
                with pe.Fori(0, WINDOWS) as w:
                    n = c * WINDOWS + w
                    pe.wait_ge(w_low, c + 1)
                    pe.wait_ge(w_onehot, n + 1)
                    pe.wait_ge(w_added, n + 1)
                    segment(0, 1, w_seg)

            sweep(pe, chunk_work, [(w_first, 1), (w_second, 1), (w_seg, WINDOWS)],
                  before=lambda: pe.wait_ge(sums_added, HALVES),
                  after=lambda: pe.wait_ge(swept, 1))
            keep_warm(4)
            pe.wait_ge(consts, 5)
            pe.wait_ge(sums_added, HALVES)
            for f in range(FINALS):
                if f >= 4:
                    pe.wait_ge(y_ready, f - 3)
                for b in range(FINAL):
                    n = f * FINAL + b
                    last = pe.matmul(folded(f)[:, b * D:b * D + FOLD], sums[:, n * P:(n + 1) * P], fold[:, :],
                                     start=True, stop=True, skip_group_check=True)
                last.then_inc(fold_done, 1)


def kernel(x, src, dst, edge_attr_64, L0_gnn_W1, L0_gnn_b1, L0_gnn_W2, L0_gnn_b2,
           L0_gnn_G1, L0_gnn_g1, L0_gnn_G2, L0_gnn_g2):
    import concourse.bacc as bacc
    from concourse.bass_utils import run_bass_kernel_spmd

    f32 = np.float32
    e = np.zeros((CHUNKS * CHUNK, D), f32)
    e[:EDGES] = np.asarray(edge_attr_64)
    d = np.full((CHUNKS * CHUNK,), NODES, np.int32)
    d[:EDGES] = np.asarray(dst)
    n = np.zeros((NODES_PAD, D), f32)
    n[:NODES] = np.asarray(x)
    w1g1 = np.concatenate([np.asarray(L0_gnn_W1), np.asarray(L0_gnn_G1)], 1)
    w2g2 = np.zeros((P, P), f32)
    w2g2[:D, :D], w2g2[D:, D:] = np.asarray(L0_gnn_W2), np.asarray(L0_gnn_G2)
    arrays = {
        "x_nodes": n.reshape(BLOCKS, P, D).transpose(1, 0, 2),
        "x_edges": e.reshape(CHUNKS, 2, HALF, D).transpose(1, 3, 0, 2).reshape(P, CHUNKS, HALF),
        "dst_halves": d.reshape(HALF_ROWS, HALF_COLS, HALF),
        "dst_tiles": d.reshape(HALVES, TILES, TILE).transpose(2, 0, 1),
        "w_first": np.concatenate([w1g1, w1g1], 0),
        "w_second": w2g2,
        "b_first": np.concatenate([np.asarray(L0_gnn_b1), np.asarray(L0_gnn_g1)]).reshape(P, 1),
        "b_second": np.concatenate([np.asarray(L0_gnn_b2), np.asarray(L0_gnn_g2)]).reshape(1, P),
    }
    arrays = {k: np.ascontiguousarray(v) for k, v in arrays.items()}
    nc = bacc.Bacc("TRN2", target_bir_lowering=False, num_devices=1)
    args = [nc.dram_tensor(k, v.shape, mybir.dt.from_np(v.dtype), kind="ExternalInput").ap()
            for k, v in arrays.items()]
    out = nc.dram_tensor("out", (P, BLOCKS, D), mybir.dt.float32, kind="ExternalOutput").ap()
    build(nc, *args, out)
    r = run_bass_kernel_spmd(nc, [arrays], core_ids=[0])
    return np.ascontiguousarray(r.results[0]["out"].transpose(1, 0, 2).reshape(NODES_PAD, D)[:NODES])
```
